# Optimizing a Trainium2 kernel written in Bass

```python
import numpy as np
import jax
import jax.numpy as jnp

def _softmax(x, axis=-1):
    return jax.nn.softmax(x, axis=axis)

def _gelu(x):
    return jax.nn.gelu(x, approximate=True)

def _silu(x):
    return jax.nn.silu(x)

def _sigmoid(x):
    return jax.nn.sigmoid(x)

def _layernorm(x, axis=-1, eps=1e-05):
    m = jnp.mean(x, axis=axis, keepdims=True)
    v = jnp.var(x, axis=axis, keepdims=True)
    return (x - m) / jnp.sqrt(v + eps)

def _scatter_add(tgt, idx, src, axis=0):
    return tgt.at[idx].add(src)

def _segment_sum(src, seg, n):
    return jax.ops.segment_sum(src, seg, n)
kernel_name = 'mk_adj_preln_d1_adj_r2_d9f50c'

def setup_inputs(seed: int=0):
    np.random.seed(seed)
    _w = jnp.asarray

    def _rec_inputs():
        import jax
        import jax.numpy as jnp
        _gk = jax.random.key(seed)
        x = -0.000929 + 1 * jax.random.normal(jax.random.fold_in(_gk, 1), (8192, 64), jnp.float32)
        _a = jax.random.bernoulli(jax.random.fold_in(_gk, 2), 0.000488281, (8192, 8192))
        _a = jnp.logical_or(_a, jnp.swapaxes(_a, -1, -2))
        _a = jnp.logical_or(_a, jnp.eye(8192, dtype=bool))
        _af = _a.astype(jnp.float32)
        adj = _af
        return (x, adj)
    x, adj = _rec_inputs()

    def _L0_gnn_setup():
        import jax, jax.numpy as jnp
        import numpy as np
        N = 8192
        D_IN = 64
        D_OUT = 64
        EDGE_P = 0.002
        key = jax.random.key(seed)
        kx, ka, kw = jax.random.split(key, 3)
        X = jax.random.normal(kx, (N, D_IN), dtype=jnp.float32)
        adj = (jax.random.uniform(ka, (N, N)) < EDGE_P).astype(jnp.float32)
        W = jax.random.normal(kw, (D_OUT, 2 * D_IN), dtype=jnp.float32) * (1.0 / np.sqrt(2 * D_IN))
        return {'X': X, 'adj': adj, 'W': W}
    _L0_gnn_all = _L0_gnn_setup()
    _L0_gnn_in = {k: v for k, v in _L0_gnn_all.items() if k in ('W',)}
    del _L0_gnn_all
    return {'x': x, 'adj': adj, 'L0_gnn_W': _L0_gnn_in['W']}

def reference(x, adj, L0_gnn_W):
    import jax
    import jax.numpy as jnp

    def _L0_gnn_ref(X, adj, W):
        import jax, jax.numpy as jnp
        import numpy as np
        N = 8192
        D_IN = 64
        D_OUT = 64
        EDGE_P = 0.002
        deg = jnp.sum(adj, axis=1, keepdims=True)
        nb_agg = adj @ X / jnp.maximum(deg, 1.0)
        X_cat = jnp.concatenate([X, nb_agg], axis=1)
        out = X_cat @ W.T
        return jax.nn.relu(out)
    h = jnp.maximum(_layernorm(x, axis=-1), 0.0)
    x = x + _L0_gnn_ref(h, adj, L0_gnn_W)
    return x

_drawn_inputs = setup_inputs


def setup_inputs(seed=0):
    import zlib

    import numpy as np

    out = dict(_drawn_inputs(seed))
    spreads = {}
    factors = {}
    for name, (base, spread) in spreads.items():
        noise = np.random.default_rng([zlib.crc32(name.encode()), seed]).standard_normal(out[name].shape)
        drawn = base * np.exp(spread * noise) if base else spread * noise
        out[name] = jnp.asarray(drawn.astype(out[name].dtype))
    for name, factor in factors.items():
        out[name] = (out[name] * factor).astype(out[name].dtype)
    return out
```

```python
import concourse.bass as bass
from concourse import mybir
from contextlib import ExitStack




def gnn_layer(nc: bass.Bass, x: bass.AP, adj: bass.AP, w: bass.AP, out: bass.AP):
    F32 = mybir.dt.float32
    ALU = mybir.AluOpType
    ACT = mybir.ActivationFunctionType
    AX = mybir.AxisListType

    P = 128
    D = w.shape[1]
    NT = x.shape[1] // D
    NG, NP, _, T, _ = adj.shape
    C = adj.shape[4] // 2
    RING = 16
    REUSE = NP // RING
    CH = 4
    CT = NT // CH
    CW = CT * D
    BPC = CW // C
    MPB = C // P
    EPS = 1e-5
    STEPS = 3

    ctx = ExitStack()
    with ctx:
        def sb(name, shape):
            return ctx.enter_context(nc.sbuf_tensor(name, shape, F32))

        def bank(name):
            return ctx.enter_context(nc.psum_tensor(name, [P, C], F32))

        def sem(name):
            return ctx.enter_context(nc.semaphore(name))

        ring = sb("ring", [P, RING, T, 2 * C])
        acc = sb("acc", [P, T, 2 * C])
        proj = sb("proj", [P, NT * D])
        h_t = sb("h_t", [P, NT * D])
        x_t = sb("x_t", [P, NT * D])
        agg_sb = sb("agg_sb", [P, C])
        deg_sb = sb("deg_sb", [P, C])
        ident = sb("ident", [P, P])
        ones = sb("ones", [P, D])
        w1 = sb("w1", [P, P])
        w2 = sb("w2", [P, P])
        neg_mean = sb("neg_mean", [P, NT])
        var = sb("var", [P, NT])
        std = sb("std", [P, NT])
        rstd = sb("rstd", [P, NT])
        corr = sb("corr", [P, NT])

        SQ_SLOT, H_SLOT, X_SLOT = RING - 5, RING - 4, RING - 2
        flat = ring[:, :, :, :].rearrange("p s t c -> p (s t c)")
        SLOT = T * 2 * C
        x_n = flat[:, X_SLOT * SLOT:X_SLOT * SLOT + NT * D]
        h_n = flat[:, H_SLOT * SLOT:H_SLOT * SLOT + NT * D]
        sq = flat[:, SQ_SLOT * SLOT:SQ_SLOT * SLOT + 2 * CW]

        agg = bank("agg")
        deg = bank("deg")
        x_tr = [bank(f"x_tr{i}") for i in range(BPC)]
        h_tr = [bank(f"h_tr{i}") for i in range(BPC)]
        p_mm = [bank(f"p_mm{i}") for i in range(BPC)]
        root = x_tr[0]

        x_landed = [sem(f"x_landed{c}") for c in range(CH)]
        w_landed = sem("w_landed")
        slot_landed = [sem(f"slot_landed{s}") for s in range(RING)]
        w_zeroed = sem("w_zeroed")
        ident_zeroed = sem("ident_zeroed")
        consts_ready = sem("consts_ready")
        ln_chain = sem("ln_chain")
        centred = sem("centred")
        squared = sem("squared")
        var_ready = sem("var_ready")
        std_ready = sem("std_ready")
        h_ready = sem("h_ready")
        x_transposed = sem("x_transposed")
        h_transposed = sem("h_transposed")
        projected = sem("projected")
        x_t_ready = sem("x_t_ready")
        h_t_ready = sem("h_t_ready")
        proj_ready = sem("proj_ready")
        pieces_used = sem("pieces_used")
        pieces_added = sem("pieces_added")
        deg_ready = sem("deg_ready")
        root_ready = sem("root_ready")
        agg_read = sem("agg_read")
        finish_chain = sem("finish_chain")
        out_ready = sem("out_ready")
        out_stored = sem("out_stored")

        block = ctx.enter_context(nc.Block())

        def landed(k, g):
            return (g * REUSE + (k // RING + 1)) * 16

        @block.sync
        def _(sp):
            for c in range(CH):
                sp.dma_start(x_n[:, c * CW:(c + 1) * CW], x[:, c * CW:(c + 1) * CW]).then_inc(x_landed[c], 16)
            for k in range(RING):
                if k == SQ_SLOT:
                    sp.wait_ge(var_ready, CH)
                if k == H_SLOT:
                    sp.wait_ge(h_transposed, CH * BPC)
                if k == X_SLOT:
                    sp.wait_ge(x_transposed, CH * BPC)
                sp.dma_start(ring[:, k, :, :], adj[0, k]).then_inc(slot_landed[k], 16)

            def reload(slot_k, g, src):
                through = g * NP + (slot_k + 1)
                sp.wait_ge(pieces_used, through)
                if slot_k < NP - 1:
                    sp.wait_ge(pieces_added, through)
                s = slot_k % RING
                sp.dma_start(ring[:, s, :, :], src).then_inc(slot_landed[s], 16)

            with sp.Fori(0, NG - 1) as g:
                for k in range(RING, NP):
                    reload(k - RING, g, adj[g, k])
                for k in range(RING):
                    reload(k + NP - RING, g, adj[g + 1, k])
            for k in range(RING, NP):
                reload(k - RING, NG - 1, adj[NG - 1, k])

        @block.gpsimd
        def _(pool):
            nc.gpsimd.memset(w1[:, :], 0.0)
            nc.gpsimd.memset(w2[:, :], 0.0).then_inc(w_zeroed, 1)
            nc.gpsimd.memset(ones[:, :], 1.0)
            nc.gpsimd.memset(ident[:, :], 0.0).then_inc(ident_zeroed, 1)
            pool.wait_ge(ident_zeroed, 1)
            nc.gpsimd.affine_select(out=ident[:, :], in_=ident[:, :], compare_op=ALU.not_equal, fill=1.0, base=0,
                                    pattern=[[-1, P]], channel_multiplier=1).then_inc(consts_ready, 1)

        @block.scalar
        def _(act):
            act.wait_ge(w_zeroed, 1)
            for half in range(2):
                q = slice(half * D, (half + 1) * D)
                act.dma_start(w1[q, q], w[0:D, :]).then_inc(w_landed, 16)
                act.dma_start(w2[q, q], w[D:2 * D, :]).then_inc(w_landed, 16)

            def square(c):
                act.wait_ge(centred, c + 1)
                if c >= 2:
                    act.wait_ge(var_ready, c - 1)
                nc.scalar.activation(sq[:, c % 2 * CW:(c % 2 + 1) * CW], h_n[:, c * CW:(c + 1) * CW],
                                     ACT.Square).then_inc(squared, 1)

            def root_of_var(c):
                act.wait_ge(var_ready, c + 1)
                nc.scalar.activation(std[:, c * CT:(c + 1) * CT], var[:, c * CT:(c + 1) * CT],
                                     ACT.Sqrt).then_inc(std_ready, 1)

            def copy_out(c, filled, banks, dst, done):
                for b in range(BPC):
                    act.wait_ge(filled, c * BPC + b + 1)
                    at = c * CW + b * C
                    nc.scalar.copy(dst[:, at:at + C], banks[b][:, :]).then_inc(done, 1)

            def x_out(c):
                copy_out(c, x_transposed, x_tr, x_t, x_t_ready)

            def h_out(c):
                copy_out(c, h_transposed, h_tr, h_t, h_t_ready)

            def p_out(c):
                copy_out(c, projected, p_mm, proj, proj_ready)

            square(0)
            x_out(0)
            square(1)
            root_of_var(0)
            square(2)
            root_of_var(1)
            h_out(0)
            p_out(0)
            x_out(1)
            square(3)
            root_of_var(2)
            h_out(1)
            p_out(1)
            x_out(2)
            root_of_var(3)
            h_out(2)
            p_out(2)
            x_out(3)
            h_out(3)
            p_out(3)

            with act.Fori(0, NG) as g:
                act.wait_ge(pieces_used, g * NP + NP)
                nc.scalar.copy(agg_sb[:, :], agg[:, :]).then_inc(agg_read, 1)
                act.wait_ge(out_ready, g + 1)
                act.dma_start(out[g], x_t[:, bass.ts(g, C)]).then_inc(out_stored, 16)
            act.wait_ge(out_stored, 16 * NG)

        @block.vector
        def _(dve):
            chain = [0]

            def step(ins):
                chain[0] += 1
                ins.then_inc(ln_chain, 1)
                dve.wait_ge(ln_chain, chain[0])

            def view(t, c):
                return t[:, c * CW:(c + 1) * CW].rearrange("p (t f) -> p t f", f=D)

            def over_features(t, c):
                return t[:, c * CT:(c + 1) * CT].unsqueeze(2).to_broadcast([P, CT, D])

            def centre(c):
                dve.wait_ge(x_landed[c], 16)
                m = neg_mean[:, c * CT:(c + 1) * CT]
                step(nc.vector.tensor_reduce(m, view(x_n, c), AX.X, ALU.add))
                step(nc.vector.tensor_scalar(m, m, -1.0 / D, None, ALU.mult))
                nc.vector.tensor_tensor(view(h_n, c), view(x_n, c), over_features(neg_mean, c),
                                        ALU.add).then_inc(centred, 1)

            def variance(c):
                dve.wait_ge(squared, c + 1)
                v = var[:, c * CT:(c + 1) * CT]
                s = sq[:, c % 2 * CW:(c % 2 + 1) * CW].rearrange("p (t f) -> p t f", f=D)
                step(nc.vector.tensor_reduce(v, s, AX.X, ALU.add))
                nc.vector.tensor_scalar(v, v, 1.0 / D, EPS, ALU.mult, ALU.add).then_inc(var_ready, 1)

            def normalise(c):
                dve.wait_ge(std_ready, c + 1)
                q = slice(c * CT, (c + 1) * CT)
                step(nc.vector.reciprocal(rstd[:, q], std[:, q]))
                step(nc.vector.tensor_tensor(corr[:, q], rstd[:, q], rstd[:, q], ALU.mult))
                step(nc.vector.tensor_tensor(corr[:, q], corr[:, q], var[:, q], ALU.mult))
                step(nc.vector.tensor_scalar(corr[:, q], corr[:, q], -0.5, 1.5, ALU.mult, ALU.add))
                step(nc.vector.tensor_tensor(rstd[:, q], rstd[:, q], corr[:, q], ALU.mult))
                nc.vector.scalar_tensor_tensor(view(h_n, c), view(h_n, c), 0.0, over_features(rstd, c),
                                               ALU.max, ALU.mult).then_inc(h_ready, 1)

            centre(0)
            centre(1)
            variance(0)
            centre(2)
            normalise(0)
            variance(1)
            centre(3)
            normalise(1)
            variance(2)
            normalise(2)
            variance(3)
            normalise(3)

            with dve.Fori(0, NG) as g:
                dve.wait_ge(slot_landed[0], landed(0, g))
                dve.wait_ge(slot_landed[1], landed(1, g))
                nc.vector.tensor_tensor(acc[:, :, :], ring[:, 0, :, :], ring[:, 1, :, :],
                                        ALU.add).then_inc(pieces_added, 2)
                for k in range(2, NP - 1):
                    dve.wait_ge(slot_landed[k % RING], landed(k, g))
                    dve.wait_ge(pieces_added, g * NP + k)
                    nc.vector.tensor_tensor(acc[:, :, :], acc[:, :, :], ring[:, k % RING, :, :],
                                            ALU.add).then_inc(pieces_added, 1)

                dve.wait_ge(deg_ready, g + 1)
                nc.vector.tensor_scalar(deg_sb[:, :], deg[:, :], 1.0, None, ALU.max).then_inc(pieces_added, 1)
                dve.wait_ge(pieces_added, g * NP + NP)
                nc.vector.reciprocal(deg_sb[:, :], deg_sb[:, :]).then_inc(finish_chain, 1)
                dve.wait_ge(finish_chain, g * STEPS + 1)
                dve.wait_ge(agg_read, g + 1)
                nc.vector.tensor_tensor(deg_sb[:, :], agg_sb[:, :], deg_sb[:, :], ALU.mult).then_inc(finish_chain, 1)
                dve.wait_ge(finish_chain, g * STEPS + 2)
                dve.wait_ge(root_ready, g + 1)
                nc.vector.tensor_tensor(deg_sb[:, :], deg_sb[:, :], root[:, :], ALU.add).then_inc(finish_chain, 1)
                dve.wait_ge(finish_chain, g * STEPS + 3)
                here = x_t[:, bass.ts(g, C)]
                nc.vector.scalar_tensor_tensor(here, deg_sb[:, :], 0.0, here, ALU.max, ALU.add).then_inc(out_ready, 1)

        @block.tensor
        def _(pe):
            pe.wait_ge(consts_ready, 1)

            def transposes(c, src, banks, done, copied):
                for b in range(BPC):
                    if c >= 1:
                        pe.wait_ge(copied, (c - 1) * BPC + b + 1)
                    for i in range(MPB):
                        at = c * CW + (b * MPB + i) * P
                        last = nc.tensor.transpose(banks[b][:, i * P:(i + 1) * P], src[:, at:at + P], ident[:, :])
                    last.then_inc(done, 1)

            def project(c):
                for b in range(BPC):
                    pe.wait_ge(h_t_ready, c * BPC + b + 1)
                    if c >= 1:
                        pe.wait_ge(proj_ready, (c - 1) * BPC + b + 1)
                    for i in range(MPB):
                        at = c * CW + (b * MPB + i) * P
                        last = nc.tensor.matmul(p_mm[b][:, i * P:(i + 1) * P], h_t[:, at:at + P], w2[:, :],
                                                start=True, stop=True)
                    last.then_inc(projected, 1)

            for c in range(CH):
                pe.wait_ge(x_landed[c], 16)
                transposes(c, x_n, x_tr, x_transposed, x_t_ready)
                pe.wait_ge(h_ready, c + 1)
                transposes(c, h_n, h_tr, h_transposed, h_t_ready)
                if c == 0:
                    pe.wait_ge(w_landed, 64)
                project(c)
            pe.wait_ge(x_t_ready, CH * BPC)
            pe.wait_ge(proj_ready, CH * BPC)

            def aggregate(k):
                for t in range(T):
                    tile = k * T + t
                    for half in range(2):
                        last = nc.tensor.matmul(agg[half * D:(half + 1) * D, :], proj[:, tile * D:(tile + 1) * D],
                                                ring[:, k % RING, t, half * C:(half + 1) * C],
                                                start=(tile == 0), stop=(tile == NT - 1))
                last.then_inc(pieces_used, 1)

            def degrees(src, first, final):
                for t in range(T):
                    for half in range(2):
                        last = nc.tensor.matmul(deg[half * D:(half + 1) * D, :], ones[:, :],
                                                src[:, t, half * C:(half + 1) * C],
                                                start=(first and t == 0), stop=(final and t == T - 1))
                return last

            with pe.Fori(0, NG) as g:
                for k in range(NP - 1):
                    pe.wait_ge(slot_landed[k % RING], landed(k, g))
                    aggregate(k)
                pe.wait_ge(pieces_added, g * NP + (NP - 1))
                nc.tensor.matmul(root[:, :], w1[:, :], h_t[:, bass.ts(g, C)], start=True,
                                 stop=True).then_inc(root_ready, 1)
                degrees(acc, True, False)
                pe.wait_ge(slot_landed[(NP - 1) % RING], landed(NP - 1, g))
                degrees(ring[:, (NP - 1) % RING, :, :], False, True).then_inc(deg_ready, 1)
                aggregate(NP - 1)
                pe.wait_ge(agg_read, g + 1)


def kernel(x, adj, L0_gnn_W):
    import numpy as np
    import concourse.bacc as bacc
    from concourse import mybir
    from concourse.bass_utils import run_bass_kernel_spmd

    n, d = x.shape
    rows, halves, pairs, per_piece = 128, 2, 4, 2
    tiles = n // rows
    groups, pieces = tiles // (halves * pairs), tiles // per_piece
    a = np.asarray(adj).reshape(rows, groups, pairs, halves, rows, pieces, per_piece)
    arrays = {
        "x": np.ascontiguousarray(np.asarray(x).reshape(rows, tiles * d)),
        "adj": np.ascontiguousarray(a.transpose(1, 5, 4, 6, 3, 2, 0)).reshape(
            groups, pieces, rows, per_piece, halves * pairs * rows),
        "w": np.ascontiguousarray(np.asarray(L0_gnn_W).T),
    }
    nc = bacc.Bacc("TRN2", target_bir_lowering=False, num_devices=1)
    aps = {k: nc.dram_tensor(k, v.shape, mybir.dt.from_np(v.dtype), kind="ExternalInput").ap()
           for k, v in arrays.items()}
    out = nc.dram_tensor("out", (groups, halves * d, pairs * rows), mybir.dt.float32, kind="ExternalOutput").ap()
    gnn_layer(nc, aps["x"], aps["adj"], aps["w"], out)
    r = run_bass_kernel_spmd(nc, [arrays], core_ids=[0])
    y = r.results[0]["out"].reshape(groups, halves, d, pairs, rows)
    return np.ascontiguousarray(y.transpose(4, 0, 3, 1, 2)).reshape(n, d)
```
